# Optimizing a Trainium2 kernel written in Bass

```python
import numpy as np
import jax
import jax.numpy as jnp

def _softmax(x, axis=-1):
    return jax.nn.softmax(x, axis=axis)

def _gelu(x):
    return jax.nn.gelu(x, approximate=True)

def _silu(x):
    return jax.nn.silu(x)

def _sigmoid(x):
    return jax.nn.sigmoid(x)

def _layernorm(x, axis=-1, eps=1e-05):
    m = jnp.mean(x, axis=axis, keepdims=True)
    v = jnp.var(x, axis=axis, keepdims=True)
    return (x - m) / jnp.sqrt(v + eps)

def _scatter_add(tgt, idx, src, axis=0):
    return tgt.at[idx].add(src)

def _segment_sum(src, seg, n):
    return jax.ops.segment_sum(src, seg, n)
kernel_name = 'mk_gnn_preln_d1_gnn_r16_0e191d'

def setup_inputs(seed: int=0):
    np.random.seed(seed)
    _w = jnp.asarray

    def _rec_inputs():
        import jax
        import jax.numpy as jnp
        _gk = jax.random.key(seed)
        x = -0.000364 + 1 * jax.random.normal(jax.random.fold_in(_gk, 1), (3125, 768), jnp.float32)
        _s = jax.random.randint(jax.random.fold_in(_gk, 2), (25000,), 0, 3125, jnp.int32)
        _d = jax.random.randint(jax.random.fold_in(_gk, 3), (25000,), 0, 3125, jnp.int32)
        _loop = jnp.arange(3125, dtype=jnp.int32)
        src = jnp.concatenate([_s, _d, _loop])
        dst = jnp.concatenate([_d, _s, _loop])
        _o = jnp.argsort(dst, stable=True)
        src = src[_o]
        dst = dst[_o]
        return (x, src, dst)
    x, src, dst = _rec_inputs()

    def _L0_gnn_setup():
        import jax, jax.numpy as jnp
        import numpy as np
        N_NODES = 1250
        N_EDGES = 10000
        IN_DIM = 768
        HID = 256
        HEADS = 4
        OUT_DIM = 768
        LN_EPS = 1e-05

        def _add_self_loops(edge_index, n):
            loop = jnp.arange(n, dtype=edge_index.dtype)
            return jnp.concatenate([edge_index, jnp.stack([loop, loop])], axis=1)

        def gat_conv(x, edge_index, W, a_src, a_dst, bias, heads, out_ch, concat):
            n = x.shape[0]
            ei = _add_self_loops(edge_index, n)
            src, dst = (ei[0], ei[1])
            xl = (x @ W).reshape(n, heads, out_ch)
            alpha_src = jnp.einsum('nhc,hc->nh', xl, a_src)
            alpha_dst = jnp.einsum('nhc,hc->nh', xl, a_dst)
            e = jax.nn.leaky_relu(alpha_src[src] + alpha_dst[dst], 0.2)
            m = jax.ops.segment_max(e, dst, num_segments=n)
            e = jnp.exp(e - m[dst])
            s = jax.ops.segment_sum(e, dst, num_segments=n)
            alpha = e / (s[dst] + 1e-16)
            msg = xl[src] * alpha[:, :, None]
            out = jax.ops.segment_sum(msg, dst, num_segments=n)
            out = out.reshape(n, heads * out_ch) if concat else out.mean(axis=1)
            return out + bias

        def layer_norm(x, g, b):
            mu = jnp.mean(x, axis=-1, keepdims=True)
            var = jnp.var(x, axis=-1, keepdims=True)
            return (x - mu) * jax.lax.rsqrt(var + LN_EPS) * g + b
        key = jax.random.key(seed)
        ks = jax.random.split(key, 16)
        s = 0.02
        HC = HID * HEADS
        return {'x': jax.random.normal(ks[0], (N_NODES, IN_DIM), jnp.float32), 'edge_index': jax.random.randint(ks[1], (2, N_EDGES), 0, N_NODES, jnp.int64 if jax.config.jax_enable_x64 else jnp.int32), 'W1': jax.random.normal(ks[2], (IN_DIM, HC), jnp.float32) * s, 'a_src1': jax.random.normal(ks[3], (HEADS, HID), jnp.float32) * s, 'a_dst1': jax.random.normal(ks[4], (HEADS, HID), jnp.float32) * s, 'b1': jnp.zeros((HC,), jnp.float32), 'g1': jnp.ones((HC,), jnp.float32), 'be1': jnp.zeros((HC,), jnp.float32), 'Wr1': jax.random.normal(ks[5], (IN_DIM, HC), jnp.float32) * s, 'br1': jnp.zeros((HC,), jnp.float32), 'W2': jax.random.normal(ks[6], (HC, OUT_DIM), jnp.float32) * s, 'a_src2': jax.random.normal(ks[7], (1, OUT_DIM), jnp.float32) * s, 'a_dst2': jax.random.normal(ks[8], (1, OUT_DIM), jnp.float32) * s, 'b2': jnp.zeros((OUT_DIM,), jnp.float32), 'g2': jnp.ones((OUT_DIM,), jnp.float32), 'be2': jnp.zeros((OUT_DIM,), jnp.float32), 'Wr2': jax.random.normal(ks[9], (HC, OUT_DIM), jnp.float32) * s, 'br2': jnp.zeros((OUT_DIM,), jnp.float32)}
    _L0_gnn_all = _L0_gnn_setup()
    _L0_gnn_in = {k: v for k, v in _L0_gnn_all.items() if k in ('W1', 'a_src1', 'a_dst1', 'b1', 'g1', 'be1', 'Wr1', 'br1', 'W2', 'a_src2', 'a_dst2', 'b2', 'g2', 'be2', 'Wr2', 'br2')}
    del _L0_gnn_all
    return {'x': x, 'src': src, 'dst': dst, 'L0_gnn_W1': _L0_gnn_in['W1'], 'L0_gnn_a_src1': _L0_gnn_in['a_src1'], 'L0_gnn_a_dst1': _L0_gnn_in['a_dst1'], 'L0_gnn_b1': _L0_gnn_in['b1'], 'L0_gnn_g1': _L0_gnn_in['g1'], 'L0_gnn_be1': _L0_gnn_in['be1'], 'L0_gnn_Wr1': _L0_gnn_in['Wr1'], 'L0_gnn_br1': _L0_gnn_in['br1'], 'L0_gnn_W2': _L0_gnn_in['W2'], 'L0_gnn_a_src2': _L0_gnn_in['a_src2'], 'L0_gnn_a_dst2': _L0_gnn_in['a_dst2'], 'L0_gnn_b2': _L0_gnn_in['b2'], 'L0_gnn_g2': _L0_gnn_in['g2'], 'L0_gnn_be2': _L0_gnn_in['be2'], 'L0_gnn_Wr2': _L0_gnn_in['Wr2'], 'L0_gnn_br2': _L0_gnn_in['br2']}

def reference(x, src, dst, L0_gnn_W1, L0_gnn_a_src1, L0_gnn_a_dst1, L0_gnn_b1, L0_gnn_g1, L0_gnn_be1, L0_gnn_Wr1, L0_gnn_br1, L0_gnn_W2, L0_gnn_a_src2, L0_gnn_a_dst2, L0_gnn_b2, L0_gnn_g2, L0_gnn_be2, L0_gnn_Wr2, L0_gnn_br2):
    import jax
    import jax.numpy as jnp

    def _L0_gnn_ref(x, edge_index, W1, a_src1, a_dst1, b1, g1, be1, Wr1, br1, W2, a_src2, a_dst2, b2, g2, be2, Wr2, br2):
        import jax, jax.numpy as jnp
        import numpy as np
        N_NODES = 1250
        N_EDGES = 10000
        IN_DIM = 768
        HID = 256
        HEADS = 4
        OUT_DIM = 768
        LN_EPS = 1e-05

        def _add_self_loops(edge_index, n):
            loop = jnp.arange(n, dtype=edge_index.dtype)
            return jnp.concatenate([edge_index, jnp.stack([loop, loop])], axis=1)

        def gat_conv(x, edge_index, W, a_src, a_dst, bias, heads, out_ch, concat):
            n = x.shape[0]
            ei = _add_self_loops(edge_index, n)
            src, dst = (ei[0], ei[1])
            xl = (x @ W).reshape(n, heads, out_ch)
            alpha_src = jnp.einsum('nhc,hc->nh', xl, a_src)
            alpha_dst = jnp.einsum('nhc,hc->nh', xl, a_dst)
            e = jax.nn.leaky_relu(alpha_src[src] + alpha_dst[dst], 0.2)
            m = jax.ops.segment_max(e, dst, num_segments=n)
            e = jnp.exp(e - m[dst])
            s = jax.ops.segment_sum(e, dst, num_segments=n)
            alpha = e / (s[dst] + 1e-16)
            msg = xl[src] * alpha[:, :, None]
            out = jax.ops.segment_sum(msg, dst, num_segments=n)
            out = out.reshape(n, heads * out_ch) if concat else out.mean(axis=1)
            return out + bias

        def layer_norm(x, g, b):
            mu = jnp.mean(x, axis=-1, keepdims=True)
            var = jnp.var(x, axis=-1, keepdims=True)
            return (x - mu) * jax.lax.rsqrt(var + LN_EPS) * g + b
        h0 = x
        h = gat_conv(x, edge_index, W1, a_src1, a_dst1, b1, HEADS, HID, True)
        h = layer_norm(h, g1, be1)
        h = jax.nn.relu(h)
        h = h + (h0 @ Wr1 + br1)
        h1 = h
        h = gat_conv(h, edge_index, W2, a_src2, a_dst2, b2, 1, OUT_DIM, False)
        h = layer_norm(h, g2, be2)
        h = h + (h1 @ Wr2 + br2)
        return h
    edge_index = jnp.stack([src, dst])
    h = jnp.maximum(_layernorm(x, axis=-1), 0.0)
    x = x + _L0_gnn_ref(h, edge_index, L0_gnn_W1, L0_gnn_a_src1, L0_gnn_a_dst1, L0_gnn_b1, L0_gnn_g1, L0_gnn_be1, L0_gnn_Wr1, L0_gnn_br1, L0_gnn_W2, L0_gnn_a_src2, L0_gnn_a_dst2, L0_gnn_b2, L0_gnn_g2, L0_gnn_be2, L0_gnn_Wr2, L0_gnn_br2)
    return x

_drawn_inputs = setup_inputs


def setup_inputs(seed=0):
    import zlib

    import numpy as np

    out = dict(_drawn_inputs(seed))
    spreads = {'L0_gnn_b1': (0.0, 0.1),
     'L0_gnn_g1': (1.0, 0.2),
     'L0_gnn_be1': (0.0, 0.1),
     'L0_gnn_br1': (0.0, 0.1),
     'L0_gnn_b2': (0.0, 0.1),
     'L0_gnn_g2': (1.0, 0.2),
     'L0_gnn_be2': (0.0, 0.1),
     'L0_gnn_br2': (0.0, 0.1)}
    factors = {'L0_gnn_a_src1': 6.897, 'L0_gnn_a_dst1': 8.0, 'L0_gnn_a_src2': 7.202, 'L0_gnn_a_dst2': 8.0}
    for name, (base, spread) in spreads.items():
        noise = np.random.default_rng([zlib.crc32(name.encode()), seed]).standard_normal(out[name].shape)
        drawn = base * np.exp(spread * noise) if base else spread * noise
        out[name] = jnp.asarray(drawn.astype(out[name].dtype))
    for name, factor in factors.items():
        out[name] = (out[name] * factor).astype(out[name].dtype)
    return out
```

```python
import concourse.bass as bass
from concourse import mybir
from contextlib import ExitStack

F32 = mybir.dt.float32
F32R = mybir.dt.float32r
BF16 = mybir.dt.bfloat16
F16 = mybir.dt.float16
I32 = mybir.dt.int32
ALU = mybir.AluOpType
ACT = mybir.ActivationFunctionType
AX = mybir.AxisListType
ds = bass.ds

P = 128
N = 3125
E = 53125
IN = 768
NT = -(-N // P)
LAST = N - (NT - 1) * P
NPAD = NT * P
QUAD = 4
TE = -(-E // P)
G = TE // QUAD
TCOL = TE + QUAD
EC = 4
EPS = 1e-5
QE = QUAD * P
BIG = 1e30
MID = N // 2
assert MID < 2048
assert TE % QUAD == 0 and NT % 2 == 1 and TCOL <= EC * P and G == (NT + 1) * QUAD


class Layer:

    def __init__(self, k, heads, width):
        self.K = k
        self.H = heads
        self.W = width
        self.C = width // heads
        self.SW = width // 2


L1 = Layer(IN // P, 4, 1024)
L2 = Layer(1024 // P, 1, 768)


def gnn_kernel(nc, x, src, dst, W1, a_src1, a_dst1, b1, g1, be1, Wr1, br1,
               W2, a_src2, a_dst2, b2, g2, be2, Wr2, br2, out):
    ctx = ExitStack()
    with ctx:
        def sb(name, shape, dt=F32):
            return ctx.enter_context(nc.sbuf_tensor(name, shape, dt))

        def sem(name):
            return ctx.enter_context(nc.semaphore(name))

        def dram(name, shape):
            return nc.dram_tensor(name, shape, F32, kind="Internal").ap()

        hT_d = [dram("hT1_d", [NT, P, L1.K * P]), dram("hT2_d", [NT, P, L2.K * P])]
        xl_d = [dram("xl1_d", [NPAD, L1.W]), dram("xl2_d", [NPAD, L2.W])]
        res_d = [dram("res1_d", [NPAD, L1.W]), dram("res2_d", [NPAD, L2.W])]
        as_d = [dram("as1_d", [NPAD, L1.H]), dram("as2_d", [NPAD, L2.H])]

        logit_d = dram("logit_d", [NT, 2, P])
        max_d = [dram("max1_d", [NPAD, L1.H]), dram("max2_d", [NPAD, L2.H])]
        quad_d = dram("quad_d", [G, 5, QE])

        ident = sb("ident", [P, P])
        iota = sb("iota", [P, P])
        upper = sb("upper", [P, P])
        tbase = sb("tbase", [P, NT])
        zeros = sb("zeros", [P, 512], BF16)
        dst_e = sb("dst_e", [P, EC * P])
        src_e = sb("src_e", [P, EC * P], I32)
        lo_i = sb("lo_i", [1, NT], I32)
        groups_i = sb("groups_i", [1, NT], I32)
        off_i = sb("off_i", [1, NT], I32)
        tlo_i = sb("tlo_i", [1, G], I32)
        thi_i = sb("thi_i", [1, G], I32)
        toff_i = sb("toff_i", [1, G], I32)
        ident_h = sb("ident_h", [P, P], F16)
        node_mid = sb("node_mid", [P, NT])
        q_dst = sb("q_dst", [P, QE], F16)
        pens = sb("pens", [P, 4 * QE], BF16)
        rpens = sb("rpens", [4, 4 * P])
        uns_i = sb("uns_i", [1, 1], I32)
        wedge = sb("wedge", [P, TCOL * 4])
        att = sb("att", [P, NT * 8])
        own_log = sb("own_log", [P, NT * 8])
        own_b = sb("own_b", [P, NT * 24], BF16)
        nscr = sb("nscr", [P, NT * 8])
        spare = sb("spare", [P, QUAD + 1])
        wa = sb("wa", [P, 8 * 8])
        vec = sb("vec", [P, 4 * 1024])
        whi = sb("whi", [P, 12288], F32R)
        wlo = sb("wlo", [P, 12288], F32R)
        arena = sb("arena", [P, 11264])
        ps = [ctx.enter_context(nc.psum_tensor(f"ps{b}", [P, 512], F32)) for b in range(8)]

        fb_sems = [sem(f"fb_{m}") for m in "eT staged e_out quad_in compared nm nm_out idx found".split()]

        def load_weights(layer, Wm, Wr, a_s, a_d):
            K, H, W = layer.K, layer.H, layer.W
            tag = f"w{layer.H}"
            SL = 4
            w_in, a_in = [sem(f"{tag}_w_in{s}") for s in range(SL)], sem(tag + "_a_in")
            hi_done, split, split_lo = sem(tag + "_hi"), sem(tag + "_split"), sem(tag + "_split_lo")
            wst = [arena[:, s * 2048:s * 2048 + 2 * W] for s in range(SL)]
            avec = vec[:, 0:2 * W]
            prod = arena[:, SL * 2048:SL * 2048 + 2 * W]
            with nc.Block() as block:
                @block.sync
                def _(sp):
                    for n, a in enumerate((a_s, a_d)):
                        sp.dma_start(avec[:, n * W:(n + 1) * W],
                                     a.rearrange("h c -> (h c)").partition_broadcast(P)).then_inc(a_in, 16)
                    for k in range(K):
                        if k >= SL:
                            sp.wait_ge(split, k - SL + 1)
                            sp.wait_ge(split_lo, k - SL + 1)
                        sp.dma_start(wst[k % SL][:, 0:W], Wm[k * P:(k + 1) * P, :]).then_inc(w_in[k % SL], 16)
                        sp.dma_start(wst[k % SL][:, W:2 * W], Wr[k * P:(k + 1) * P, :]).then_inc(w_in[k % SL], 16)

                @block.scalar
                def _(act):
                    for k in range(K):
                        act.wait_ge(w_in[k % SL], 32 * (k // SL + 1))
                        nc.scalar.activation(whi[:, k * 2 * W:(k + 1) * 2 * W], wst[k % SL], ACT.Copy).then_inc(hi_done, 1)

                @block.vector
                def _(dve):
                    dve.wait_ge(a_in, 32)
                    for k in range(K):
                        dve.wait_ge(w_in[k % SL], 32 * (k // SL + 1))
                        nc.vector.tensor_tensor(prod.rearrange("p (n c) -> p n c", n=2),
                                                wst[k % SL][:, 0:W].unsqueeze(1).to_broadcast([P, 2, W]),
                                                avec.rearrange("p (n c) -> p n c", n=2), ALU.mult)
                        dve.drain()
                        nc.vector.tensor_reduce(wa[:, k * 8:k * 8 + 2 * H], prod.rearrange("p (h c) -> p h c", h=2 * H), AX.X, ALU.add)
                        dve.drain().then_inc(split, 1)

                @block.gpsimd
                def _(pool):
                    for k in range(K):
                        pool.wait_ge(hi_done, k + 1)
                        sl = slice(k * 2 * W, (k + 1) * 2 * W)
                        pool.tensor_tensor(wlo[:, sl], wst[k % SL], whi[:, sl].bitcast(F32), ALU.subtract).then_inc(split_lo, 1)

        def hold(pool, slot=0):
            return pool.tensor_tensor(spare[:, slot:slot + 1], spare[:, QUAD:QUAD + 1], spare[:, QUAD:QUAD + 1], ALU.mult)

        def setup():
            edge_i = arena[:, 0:2 * EC * P].bitcast(I32).rearrange("p (b c e) -> p b c e", b=2, c=EC)
            edge_f = arena[:, 1024:1024 + 2 * EC * P].rearrange("p (b c e) -> p b c e", b=2, c=EC)
            buck_i = arena[:, 2048:2048 + TE].bitcast(I32)
            buck = arena[:, 2560:2560 + TE]
            buckm = arena[:, 3072:3072 + TE]
            tmm = arena[:, 4096:4096 + 2 * QUAD]
            qmm = arena[:, 4104:4104 + 2]
            qcnt = arena[:, 4106:4107]
            ind = arena[:, 4224:4224 + NT]
            val = arena[:, 10624:10624 + 2 * QUAD * NT]
            tl = arena[:, 4480:4484]
            itile = arena[:, 4608:4608 + NT]
            gfwd = arena[:, 4700:4700 + QUAD]
            gback = arena[:, 4704:4704 + QUAD]
            rows = arena[:, 4864:4864 + 512]
            qi = arena[0:G, 5376:5376 + QE].bitcast(I32)
            qf = arena[0:G, 6400:6400 + QE]
            same = arena[0:G, 6912:6912 + 4 * QE]
            down = arena[0:G, 8960:8960 + QE]
            qrow = arena[0:4, 9472:9472 + 3 * P]
            rsame = arena[0:4, 9856:9856 + 4 * P]
            rdown = arena[0:1, 10368:10368 + P]
            q_in = sem("q_in")
            const, padded, edges_in = sem("const"), sem("padded"), sem("edges_in")
            dve_steps, pe_steps, pool1 = sem("su_dve"), sem("su_pe"), sem("su_pool")
            with nc.Block() as block:
                @block.gpsimd
                def _(pool):
                    pool.memset(spare[:, :], 0.0)
                    pool.iota(iota[:, :], [[1, P]], base=0, channel_multiplier=0,
                              allow_small_or_imprecise_dtypes=True).then_inc(const, 1)
                    pool.iota(tbase[:, :], [[P, NT]], base=0, channel_multiplier=0,
                              allow_small_or_imprecise_dtypes=True).then_inc(const, 1)
                    pool.iota(node_mid[:, :], [[P, NT]], base=-MID, channel_multiplier=1,
                              allow_small_or_imprecise_dtypes=True).then_inc(const, 1)
                    pool.iota(itile, [[1, NT]], base=0, channel_multiplier=0,
                              allow_small_or_imprecise_dtypes=True).then_inc(const, 1)
                    pool.iota(gfwd, [[1, QUAD]], base=1, channel_multiplier=QUAD,
                              allow_small_or_imprecise_dtypes=True).then_inc(const, 1)
                    pool.iota(gback, [[-1, QUAD]], base=TE, channel_multiplier=-QUAD,
                              allow_small_or_imprecise_dtypes=True).then_inc(const, 1)
                    pool.memset(ident[:, :], 0.0).then_inc(pool1, 1)
                    pool.memset(upper[:, :], 1.0).then_inc(pool1, 1)
                    pool.wait_ge(pool1, 2)
                    pool.affine_select(out=ident[:, :], in_=ident[:, :], compare_op=ALU.not_equal, fill=1.0, base=0,
                                       pattern=[[-1, P]], channel_multiplier=1).then_inc(const, 1)
                    pool.affine_select(out=upper[:, :], in_=upper[:, :], compare_op=ALU.is_gt, fill=0.0, base=0,
                                       pattern=[[1, P]], channel_multiplier=-1).then_inc(const, 1)

                @block.sync
                def _(sp):
                    sp.wait_ge(padded, 3)
                    full = (EC - 1) * P * P
                    rest = (E - full) // P
                    for b, e in enumerate((dst, src)):
                        sp.dma_start(edge_i[:, b, 0:EC - 1, :], e[0:full].rearrange("(c p e) -> p c e", p=P, e=P)).then_inc(edges_in, 16)
                        sp.dma_start(edge_i[0:rest, b, EC - 1, :],
                                     e[full:full + rest * P].rearrange("(p e) -> p e", e=P)).then_inc(edges_in, 16)
                        sp.dma_start(edge_i[rest:rest + 1, b, EC - 1, 0:E - full - rest * P],
                                     e[full + rest * P:E].unsqueeze(0)).then_inc(edges_in, 16)

                    whole = (G - 1) * QE
                    sp.dma_start(qi[0:G - 1, :], dst[0:whole].rearrange("(g e) -> g e", e=QE)).then_inc(q_in, 16)
                    sp.dma_start(qi[G - 1:G, 0:E - whole], dst[whole:E].unsqueeze(0)).then_inc(q_in, 16)

                @block.scalar
                def _(act):
                    act.wait_ge(const, 8)
                    nc.scalar.activation(ident_h[:, :], ident[:, :], ACT.Copy)

                @block.vector
                def _(dve):
                    nc.vector.memset(qi, -1).then_inc(padded, 1)
                    nc.vector.memset(edge_i[:, 0, EC - 1, :], -1).then_inc(padded, 1)
                    nc.vector.memset(edge_i[:, 1, EC - 1, :], 0).then_inc(padded, 1)
                    nc.vector.memset(zeros[:, :], 0.0)
                    nc.vector.memset(wedge[:, :], 0.0)
                    dve.wait_ge(edges_in, 6 * 16)
                    nc.vector.tensor_copy(edge_f, edge_i).then_inc(dve_steps, 1)
                    dve.wait_ge(pe_steps, 1)
                    nc.vector.tensor_copy(dst_e[:, :], ps[0][:, :])
                    dve.drain()
                    nc.vector.tensor_copy(src_e[:, :], ps[1][:, :])
                    nc.vector.tensor_copy(buckm.bitcast(I32), dst_e[:, 0:TE])
                    dve.drain()
                    nc.vector.tensor_scalar(buck_i, buckm.bitcast(I32), 7, None, ALU.arith_shift_right)
                    dve.drain()
                    nc.vector.tensor_copy(buck, buck_i)
                    dve.drain()
                    nc.vector.tensor_scalar(buckm, buck, 0.0, 65536.0, ALU.is_lt, ALU.mult)
                    dve.drain()
                    nc.vector.tensor_tensor(buckm, buckm, buck, ALU.add)
                    dve.drain()
                    dve.drain().then_inc(dve_steps, 1)
                    dve.wait_ge(pe_steps, 2)
                    dve.wait_ge(const, 8)
                    nc.vector.tensor_reduce(tmm[0:G, 0:QUAD], ps[2][0:G, :].rearrange("p (a e) -> p a e", a=QUAD), AX.X, ALU.min)
                    nc.vector.tensor_reduce(tmm[0:G, QUAD:2 * QUAD], ps[3][0:G, :].rearrange("p (a e) -> p a e", a=QUAD), AX.X, ALU.max)
                    dve.drain()
                    nc.vector.tensor_reduce(qmm[0:G, 0:1], tmm[0:G, 0:QUAD], AX.X, ALU.min)
                    nc.vector.tensor_reduce(qmm[0:G, 1:2], tmm[0:G, QUAD:2 * QUAD], AX.X, ALU.max)
                    dve.drain()
                    nc.vector.tensor_tensor(qcnt[0:G, :], qmm[0:G, 1:2], qmm[0:G, 0:1], ALU.subtract)
                    dve.drain()
                    nc.vector.tensor_scalar(qcnt[0:G, :], qcnt[0:G, :], 1.0, None, ALU.add).then_inc(dve_steps, 1)
                    for a in range(QUAD):
                        nc.vector.tensor_scalar(ind[0:G, :], itile[0:G, :], tmm[0:G, a:a + 1], None, ALU.is_ge)
                        dve.drain()
                        nc.vector.scalar_tensor_tensor(ind[0:G, :], itile[0:G, :], tmm[0:G, QUAD + a:QUAD + a + 1], ind[0:G, :], ALU.is_le, ALU.mult)
                        dve.drain()
                        nc.vector.tensor_scalar(val[0:G, a * NT:(a + 1) * NT], ind[0:G, :], gback[0:G, a:a + 1], None, ALU.mult)
                        nc.vector.tensor_scalar(val[0:G, (QUAD + a) * NT:(QUAD + a + 1) * NT], ind[0:G, :], gfwd[0:G, a:a + 1], None, ALU.mult)
                        dve.drain()
                    dve.drain().then_inc(dve_steps, 1)
                    dve.wait_ge(pe_steps, 4)
                    nc.vector.tensor_reduce(tl[0:NT, 0:1], ps[4][0:NT, 0:QUAD * G], AX.X, ALU.max)
                    nc.vector.tensor_reduce(tl[0:NT, 1:2], ps[5][0:NT, 0:QUAD * G], AX.X, ALU.max)
                    dve.drain()
                    nc.vector.tensor_scalar(tl[0:NT, 0:1], tl[0:NT, 0:1], -1.0, float(TE), ALU.mult, ALU.add)
                    dve.drain()
                    nc.vector.tensor_tensor(tl[0:NT, 2:3], tl[0:NT, 1:2], tl[0:NT, 0:1], ALU.subtract)
                    dve.drain()
                    nc.vector.tensor_scalar(tl[0:NT, 2:3], tl[0:NT, 2:3], float(QUAD - 1), 0.0, ALU.add, ALU.max)
                    dve.drain()
                    nc.vector.tensor_copy(tl[0:NT, 3:4].bitcast(I32), tl[0:NT, 2:3])
                    dve.drain()
                    nc.vector.tensor_scalar(tl[0:NT, 3:4].bitcast(I32), tl[0:NT, 3:4].bitcast(I32), QUAD.bit_length() - 1, None, ALU.arith_shift_right)
                    dve.drain()
                    nc.vector.tensor_copy(tl[0:NT, 2:3], tl[0:NT, 3:4].bitcast(I32))
                    dve.drain()
                    nc.vector.tensor_scalar(tl[0:NT, 2:3], tl[0:NT, 2:3], 1.0, None, ALU.max).then_inc(dve_steps, 1)
                    dve.wait_ge(pe_steps, 3)
                    r2 = rows[0:1, 0:3 * P]
                    nc.vector.tensor_copy(r2.rearrange("p (b n) -> p b n", b=3)[:, :, 0:G],
                                          ps[6][0:1, 0:3 * P].rearrange("p (b n) -> p b n", b=3)[:, :, 0:G])
                    dve.drain()
                    nc.vector.tensor_copy(tlo_i[:, :], r2[:, 0:G])
                    nc.vector.tensor_scalar(thi_i[:, :], r2[:, P:P + G], 1.0, None, ALU.add)
                    nc.vector.tensor_copy(toff_i[:, :], r2[:, 2 * P:2 * P + G])
                    dve.drain()
                    dve.wait_ge(pe_steps, 5)
                    nc.vector.tensor_copy(r2.rearrange("p (b n) -> p b n", b=3)[:, :, 0:NT],
                                          ps[7][0:1, 0:3 * P].rearrange("p (b n) -> p b n", b=3)[:, :, 0:NT])
                    dve.drain()
                    for b, table in enumerate((lo_i, groups_i, off_i)):
                        nc.vector.tensor_copy(table[:, :], r2[:, b * P:b * P + NT])
                    dve.wait_ge(q_in, 32)
                    nc.vector.tensor_copy(qf, qi).then_inc(dve_steps, 1)
                    nc.vector.memset(same[:, 0:2 * QE], 0.0)
                    dve.drain()
                    nc.vector.tensor_scalar(q_dst[0:G, :], qf, float(-MID), None, ALU.add)
                    nc.vector.tensor_tensor(same[:, 1:QE], qf[:, 1:QE], qf[:, 0:QE - 1], ALU.is_equal)
                    nc.vector.tensor_tensor(same[:, QE:2 * QE - 1], qf[:, 1:QE], qf[:, 0:QE - 1], ALU.is_equal)
                    nc.vector.tensor_scalar(same[:, 2 * QE:3 * QE], qf, qf[:, 0:1], None, ALU.is_equal)
                    nc.vector.tensor_scalar(same[:, 3 * QE:4 * QE], qf, qf[:, QE - 1:QE], None, ALU.is_equal)
                    dve.drain()
                    nc.vector.tensor_scalar(pens[0:G, :], same, -1.0, BIG, ALU.add, ALU.mult)
                    nc.vector.tensor_tensor(down[:, 1:QE], qf[:, 1:QE], qf[:, 0:QE - 1], ALU.is_lt)
                    dve.drain()
                    nc.vector.scalar_tensor_tensor(down[:, 1:QE], qf[:, 1:QE], 0.0, down[:, 1:QE], ALU.is_ge, ALU.mult)
                    dve.drain()
                    nc.vector.tensor_reduce(down[:, 0:1], down[:, 1:QE], AX.X, ALU.max).then_inc(dve_steps, 1)
                    dve.wait_ge(pe_steps, 6)
                    q3 = qrow.rearrange("p (b n) -> p b n", b=3)
                    nc.vector.tensor_copy(q3[:, :, 0:G], ps[0][0:4, 0:3 * P].rearrange("p (b n) -> p b n", b=3)[:, :, 0:G])
                    nc.vector.memset(rsame, 0.0)
                    dve.drain()
                    f, l = q3[:, 0, :], q3[:, 1, :]
                    for b, (x0, x1, lo) in enumerate(((l[:, 0:G - 1], l[:, 1:G], 1), (f[:, 1:G], f[:, 0:G - 1], 0),
                                                      (l[:, 0:G - 1], f[:, 1:G], 1), (f[:, 1:G], l[:, 0:G - 1], 0))):
                        nc.vector.tensor_tensor(rsame[:, b * P + lo:b * P + lo + G - 1], x0, x1, ALU.is_equal)
                    nc.vector.tensor_tensor(rdown[:, 0:G - 1], f[0:1, 1:G], l[0:1, 0:G - 1], ALU.is_lt)
                    dve.drain()
                    nc.vector.tensor_scalar(rpens[:, :], rsame, -1.0, BIG, ALU.add, ALU.mult)
                    nc.vector.tensor_tensor(rdown[:, 0:G - 1], rdown[:, 0:G - 1], q3[0:1, 2, 0:G - 1], ALU.max)
                    dve.drain()
                    nc.vector.tensor_tensor(rdown[:, G - 2:G - 1], rdown[:, G - 2:G - 1], q3[0:1, 2, G - 1:G], ALU.max)
                    dve.drain()
                    nc.vector.tensor_reduce(rdown[:, G:G + 1], rdown[:, 0:G - 1], AX.X, ALU.max)
                    dve.drain()
                    nc.vector.tensor_copy(uns_i[:, :], rdown[:, G:G + 1])

                @block.tensor
                def _(pe):
                    pe.wait_ge(const, 8)
                    pe.wait_ge(dve_steps, 1)
                    for b in range(2):
                        for c in range(EC):
                            last = nc.tensor.transpose(ps[b][:, c * P:(c + 1) * P], edge_f[:, b, c, :], ident[:, :])
                    last.then_inc(pe_steps, 1)
                    pe.wait_ge(dve_steps, 2)
                    for b, tiles in enumerate((buckm, buck)):
                        for a in range(QUAD):
                            last = nc.tensor.transpose(ps[2 + b][0:G, a * P:(a + 1) * P],
                                                       tiles.rearrange("p (g a) -> p g a", a=QUAD)[:, :, a], ident[:, :])
                    last.then_inc(pe_steps, 1)
                    pe.wait_ge(dve_steps, 3)
                    nc.tensor.matmul(ps[6][0:1, 0:G], qmm[0:G, 0:1], ident[0:G, 0:G], start=True, stop=True)
                    nc.tensor.matmul(ps[6][0:1, P:P + G], qmm[0:G, 1:2], ident[0:G, 0:G], start=True, stop=True)
                    nc.tensor.matmul(ps[6][0:1, 2 * P:2 * P + G], qcnt[0:G, :], upper[0:G, 0:G], start=True, stop=True).then_inc(pe_steps, 1)
                    pe.wait_ge(dve_steps, 4)
                    for b in range(2):
                        for a in range(QUAD):
                            last = nc.tensor.transpose(ps[4 + b][0:NT, a * G:(a + 1) * G],
                                                       val[0:G, (b * QUAD + a) * NT:(b * QUAD + a + 1) * NT], ident[0:G, 0:G])
                    last.then_inc(pe_steps, 1)
                    pe.wait_ge(dve_steps, 5)
                    nc.tensor.matmul(ps[7][0:1, 0:NT], tl[0:NT, 0:1], ident[0:NT, 0:NT], start=True, stop=True)
                    nc.tensor.matmul(ps[7][0:1, P:P + NT], tl[0:NT, 2:3], ident[0:NT, 0:NT], start=True, stop=True)
                    nc.tensor.matmul(ps[7][0:1, 2 * P:2 * P + NT], tl[0:NT, 2:3], upper[0:NT, 0:NT], start=True, stop=True).then_inc(pe_steps, 1)
                    pe.wait_ge(dve_steps, 7)
                    for b, col in enumerate((qf[:, 0:1], qf[:, QE - 1:QE], down[:, 0:1])):
                        last = nc.tensor.transpose(ps[0][0:4, b * P:b * P + G], col.to_broadcast([G, 4]), ident[0:G, 0:G])
                    last.then_inc(pe_steps, 1)

        def inverse_root(act, st):
            nc.scalar.activation(st[:, 16:17], st[:, 13:14], ACT.Ln)
            act.drain()
            return nc.scalar.activation(st[:, 14:15], st[:, 16:17], ACT.Exp, scale=-0.5)

        def newton(dve, st):
            nc.vector.tensor_tensor(st[:, 17:18], st[:, 14:15], st[:, 14:15], ALU.mult)
            dve.drain()
            nc.vector.scalar_tensor_tensor(st[:, 17:18], st[:, 17:18], -0.5, st[:, 13:14], ALU.mult, ALU.mult)
            dve.drain()
            nc.vector.scalar_tensor_tensor(st[:, 14:15], st[:, 17:18], 1.5, st[:, 14:15], ALU.add, ALU.mult)
            dve.drain()

        def norm_input():
            K, H = L1.K, L1.H
            xb = [arena[:, s * IN:(s + 1) * IN] for s in range(2)]
            hb = [arena[:, (2 + s) * IN:(3 + s) * IN] for s in range(2)]
            hT = [arena[:, (4 + s) * IN:(5 + s) * IN] for s in range(2)]
            stat = arena[:, 6 * IN:6 * IN + 64]
            x_in = [sem(f"ni_x_in{s}") for s in range(2)]
            hT_out = [sem(f"ni_hT_out{s}") for s in range(2)]
            stats, h_ready, turned, hT_ready, logit, var_ready, inv_ready = [
                sem("ni_" + n) for n in "stats h turned hT logit var inv".split()]

            def pairs(eng, body):
                with eng.Fori(0, NT // 2) as r:
                    body(2 * r, 0, r)
                    body(2 * r + 1, 1, r)
                body(NT - 1, 0, NT // 2)

            with nc.Block() as block:
                @block.sync
                def _(sp):
                    def load(i, s, rows=P):
                        sp.dma_start(xb[s][0:rows, :], x[ds(i * P, rows), :]).then_inc(x_in[s], 16)

                    def store(i, s):
                        sp.wait_ge(hT_ready, i + 1)
                        sp.dma_start(hT_d[0][ds(i, 1), :, :].rearrange("a p n -> (a p) n"), hT[s]).then_inc(hT_out[s], 16)

                    load(0, 0)
                    load(1, 1)
                    with sp.Fori(1, NT // 2) as r:
                        for s in range(2):
                            sp.wait_ge(h_ready, 2 * r + s - 1)
                            load(2 * r + s, s)
                            store(2 * r + s - 2, s)
                    sp.wait_ge(h_ready, NT - 2)
                    load(NT - 1, 0, LAST)
                    for i in range(NT - 3, NT):
                        store(i, i % 2)
                    sp.wait_ge(hT_out[0], 16 * (NT // 2 + 2))
                    sp.wait_ge(hT_out[1], 16 * (NT // 2 + 1))

                @block.vector
                def _(dve):
                    def body(i, s, r):
                        dve.wait_ge(x_in[s], 16 * r + 16)
                        st = stat[:, 32 * s:32 * s + 32]
                        for n in range(2):
                            nc.vector.bn_stats(st[:, 6 * n:6 * n + 6], xb[s][:, n * (IN // 2):(n + 1) * (IN // 2)])
                            dve.drain()
                        nc.vector.bn_aggr(st[:, 12:14], st[:, 0:12])
                        dve.drain()
                        nc.vector.tensor_scalar(st[:, 13:14], st[:, 13:14], EPS, None, ALU.add).then_inc(var_ready, 1)
                        dve.wait_ge(inv_ready, i + 1)
                        newton(dve, st)
                        nc.vector.scalar_tensor_tensor(st[:, 15:16], st[:, 12:13], -1.0, st[:, 14:15], ALU.mult, ALU.mult).then_inc(stats, 1)
                    pairs(dve, body)

                @block.scalar
                def _(act):
                    nc.scalar.preload_act_table_set("natural_log_exp_and_others")
                    for s in range(2):
                        act.drain().then_inc(hT_out[s], 16)

                    def normalise(i, s):
                        st = stat[:, 32 * s:32 * s + 32]
                        act.wait_ge(var_ready, i + 1)
                        inverse_root(act, st).then_inc(inv_ready, 1)
                        act.wait_ge(stats, i + 1)
                        nc.scalar.activation(hb[s], xb[s], ACT.Relu, scale=st[:, 14:15], bias=st[:, 15:16]).then_inc(h_ready, 1)

                    def copy_out(i, s, r):
                        act.wait_ge(turned, i + 1)
                        act.wait_ge(hT_out[s], 16 * r + 16)
                        nc.scalar.activation(hT[s][:, 0:512], ps[2 * s][:, 0:512], ACT.Copy)
                        nc.scalar.activation(hT[s][:, 512:IN], ps[2 * s + 1][:, 0:IN - 512], ACT.Copy).then_inc(hT_ready, 1)

                    def keep_logits(i, s):
                        act.wait_ge(logit, i + 1)
                        nc.scalar.activation(att[:, ds(i * 8, 8)], ps[4 + s][:, 0:8], ACT.Copy)

                    normalise(0, 0)
                    normalise(1, 1)
                    copy_out(0, 0, 0)
                    with act.Fori(0, NT // 2 - 1) as r:
                        for s in range(2):
                            normalise(2 * r + 2 + s, s)
                            copy_out(2 * r + 1 + s, 1 - s, r + s)
                            keep_logits(2 * r + s, s)
                    normalise(NT - 1, 0)
                    copy_out(NT - 2, 1, NT // 2 - 1)
                    keep_logits(NT - 3, 0)
                    copy_out(NT - 1, 0, NT // 2)
                    keep_logits(NT - 2, 1)
                    keep_logits(NT - 1, 0)

                @block.tensor
                def _(pe):
                    def turn(i, s):
                        pe.wait_ge(h_ready, i + 1)
                        for k in range(K):
                            b = ps[2 * s + k // 4]
                            last = nc.tensor.transpose(b[:, (k % 4) * P:(k % 4 + 1) * P], hb[s][:, k * P:(k + 1) * P], ident[:, :])
                        last.then_inc(turned, 1)

                    def logits(i, s):
                        pe.wait_ge(hT_ready, i + 1)
                        for k in range(K):
                            last = nc.tensor.matmul(ps[4 + s][:, 0:2 * H], hT[s][:, k * P:(k + 1) * P],
                                                    wa[:, k * 8:k * 8 + 2 * H], start=(k == 0), stop=(k == K - 1))
                        last.then_inc(logit, 1)
                    turn(0, 0)
                    with pe.Fori(0, NT // 2) as r:
                        for s in range(2):
                            turn(2 * r + 1 + s, 1 - s)
                            logits(2 * r + s, s)
                    logits(NT - 1, 0)

        def logit_tables(layer, n):
            H = layer.H
            a4 = att[:, :].rearrange("p (t j) -> p t j", j=8)
            full = own_log[:, 0:NT * 2 * H].rearrange("p (t j) -> p t j", j=2 * H)
            parts = own_b[:, 0:NT * 6 * H].rearrange("p (t s j) -> p t s j", s=3, j=2 * H)
            rest = nscr[:, 0:NT * 2 * H].rearrange("p (t j) -> p t j", j=2 * H)
            stored = sem(f"lt{n}_stored")
            if n == 1:
                rows_in, rows_T, att_set = sem("lt_rows_in"), sem("lt_rows_T"), sem("lt_att")
                logit_rows = arena[0:2 * NT, 0:P]
            with nc.Block() as block:
                if n == 1:
                    @block.tensor
                    def _(pe):
                        pe.wait_ge(rows_in, 16)
                        nc.tensor.transpose(ps[0][:, 0:2 * NT], logit_rows, ident[0:2 * NT, 0:2 * NT]).then_inc(rows_T, 1)

                @block.vector
                def _(dve):
                    if n == 1:
                        dve.wait_ge(rows_T, 1)
                        nc.vector.tensor_copy(a4[:, :, 0:2], ps[0][:, 0:2 * NT].rearrange("p (t j) -> p t j", j=2))
                        dve.drain().then_inc(att_set, 1)
                    nc.vector.tensor_copy(full[:, :, 0:H], a4[:, :, H:2 * H])
                    nc.vector.tensor_tensor(full[:, :, H:2 * H], a4[:, :, 0:H], a4[:, :, H:2 * H], ALU.add)
                    dve.drain()
                    nc.vector.scalar_tensor_tensor(full[:, :, H:2 * H], full[:, :, H:2 * H], 0.2, full[:, :, H:2 * H], ALU.mult, ALU.max)
                    dve.drain()
                    nc.vector.tensor_copy(parts[:, :, 0, :], full)
                    dve.drain()
                    nc.vector.tensor_tensor(rest, full, parts[:, :, 0, :], ALU.subtract)
                    dve.drain()
                    nc.vector.tensor_copy(parts[:, :, 1, :], rest)
                    dve.drain()
                    nc.vector.tensor_tensor(parts[:, :, 2, :], rest, parts[:, :, 1, :], ALU.subtract)

                @block.sync
                def _(sp):
                    if n == 1:
                        sp.dma_start(logit_rows, logit_d.rearrange("t j n -> (t j) n")).then_inc(rows_in, 16)
                        sp.wait_ge(att_set, 1)
                    sp.dma_start(as_d[n].rearrange("(t p) h -> p t h", p=P), a4[:, :, 0:H],
                                 allow_slow_non_contiguous=True).then_inc(stored, 16)
                    sp.wait_ge(stored, 16)

        def project(layer, n):
            K, H, W, SW = layer.K, layer.H, layer.W, layer.SW
            KP = K * P
            hin = [arena[:, s * 1024:s * 1024 + KP] for s in range(2)]
            ost = [arena[:, 2048 + s * 512:2048 + s * 512 + SW] for s in range(4)]
            picked_e = arena[:, 4096:4096 + (TE + QUAD) * 2 * H]
            gst = [arena[:, 7456 + s * 16:7456 + s * 16 + QUAD * H].rearrange("p (a h) -> p a h", a=QUAD) for s in range(2)]
            isg = [arena[:, 7488 + s * 8:7488 + s * 8 + QUAD].bitcast(I32) for s in range(2)]
            hT_in = [sem(f"pr{n}_hT_in{s}") for s in range(2)]
            got = [[sem(f"pr{n}_got{s}{a}") for a in range(QUAD)] for s in range(2)]
            stored = [sem(f"pr{n}_stored{s}") for s in range(4)]
            (hi_ready, lo_ready, sliced, evac, idx_ready, held, spread, spread_free, ohT_ready, picked,
             pick_done, pick_free) = [sem(f"pr{n}_{m}") for m in
                                      "hi lo sliced evac idx held spread sfree ohT picked pdone pfree".split()]

            def schedule(eng, tile_quad, plain_quad=None):
                with eng.Fori(0, NT // 2) as r:
                    for slot in range(2):
                        for s in range(QUAD):
                            tile_quad(8 * r + 4 * slot + s, s % 2, 2 * r + slot, s, slot, r)
                for s in range(QUAD):
                    tile_quad(QUAD * (NT - 1) + s, s % 2, NT - 1, s, 0, NT // 2)
                if plain_quad:
                    for s in range(QUAD):
                        plain_quad(QUAD * NT + s, s % 2)

            def tiles_of(eng, g, first_tile, second, later=None):
                lo = eng.value_load(tlo_i[0:1, ds(g, 1)], min_val=0, max_val=NT - 1)
                hi = eng.value_load(thi_i[0:1, ds(g, 1)], min_val=1, max_val=NT)
                pair0 = eng.value_load(toff_i[0:1, ds(g, 1)], min_val=0, max_val=G * NT)
                first_tile(lo, pair0)
                with eng.If(hi - lo > 1):
                    if later:
                        second(start(lo + 1), pair0 + 1)
                        with eng.If(hi - lo > 2):
                            with eng.Fori(2, hi - lo) as m:
                                later(start(lo + m), pair0 + m)
                    else:
                        with eng.Fori(1, hi - lo) as m:
                            second(start(lo + m), pair0 + m)

            def start(t):
                return nc.s_assert_within(t, 0, NT - 1, skip_runtime_bounds_check_because="it is a node tile that the quad reaches")

            with nc.sbuf_tensor(f"hThi0_{n}", [P, KP], F32R) as hThi0, nc.sbuf_tensor(f"hThi1_{n}", [P, KP], F32R) as hThi1, \
                    nc.sbuf_tensor(f"hTlo0_{n}", [P, KP], F32R) as hTlo0, nc.sbuf_tensor(f"hTlo1_{n}", [P, KP], F32R) as hTlo1, \
                    nc.sbuf_tensor(f"onehotT0_{n}", [P, QE], BF16) as onehotT0, nc.sbuf_tensor(f"onehotT1_{n}", [P, QE], BF16) as onehotT1, \
                    nc.sbuf_tensor(f"onehotT2_{n}", [P, QE], BF16) as onehotT2, nc.Block() as block:
                onehotT = (onehotT0, onehotT1, onehotT2)
                hThi, hTlo = (hThi0, hThi1), (hTlo0, hTlo1)

                @block.sync
                def _(sp):
                    def load(i, slot):
                        sp.dma_start(hin[slot], hT_d[n][ds(i, 1), :, :].rearrange("a p n -> (a p) n")).then_inc(hT_in[slot], 16)

                    def tq(g, par, i, s, slot, r):
                        if s == 0 and not (isinstance(i, int) and i == NT - 1):
                            sp.wait_ge(lo_ready, i + 1)
                            load(i + 1, 1 - slot)
                        sp.wait_ge(evac, g + 1 + QUAD)
                        dest = (xl_d, res_d)[s // 2][n]
                        sp.dma_start(dest[ds(i * P, P), (s % 2) * SW:(s % 2 + 1) * SW], ost[s]).then_inc(stored[s], 16)
                    load(0, 0)
                    schedule(sp, tq)
                    for s in range(4):
                        sp.wait_ge(stored[s], 16 * (NT + 1))

                @block.gpsimd
                def _(pool):
                    def q(g, par):
                        pool.wait_ge(idx_ready, g + 1)
                        hold(pool, par).then_inc(held, 1)
                        for a in range(QUAD):
                            pool.indirect_dma_start(out=gst[par][:, a, :], out_offset=None, in_=as_d[n][:, :],
                                                    in_offset=bass.IndirectOffsetOnAxis(ap=isg[par][:, a:a + 1], axis=0)).then_inc(got[par][a], 16)
                    with pool.Fori(0, G // 2) as r:
                        for par in range(2):
                            q(2 * r + par, par)

                @block.scalar
                def _(act):
                    nc.scalar.preload_act_table_set("natural_log_exp_and_others")

                    def split_hi(i, slot, r):
                        act.wait_ge(hT_in[slot], 16 * r + 16)
                        act.wait_ge(sliced, QUAD * i)
                        nc.scalar.activation(hThi[slot][:, 0:KP], hin[slot], ACT.Copy).then_inc(hi_ready, 1)

                    def tq(g, par, i, s, slot, r):
                        if s == 2 and not (isinstance(i, int) and i == NT - 1):
                            split_hi(i + 1, 1 - slot, r + slot)
                        act.wait_ge(sliced, g + 1 + QUAD)
                        act.wait_ge(stored[s], 16 * i + 16)
                        nc.scalar.activation(ost[s], ps[s][:, 0:SW], ACT.Copy).then_inc(evac, 1)
                    act.drain().then_inc(evac, QUAD)
                    for s in range(4):
                        act.drain().then_inc(stored[s], 16)
                    act.wait_ge(hT_in[0], 16)
                    nc.scalar.activation(hThi[0][:, 0:KP], hin[0], ACT.Copy).then_inc(hi_ready, 1)
                    schedule(act, tq)

                @block.vector
                def _(dve):
                    def split_lo(i, slot):
                        dve.wait_ge(hi_ready, i + 1)
                        nc.vector.tensor_tensor(hTlo[slot][:, 0:KP], hin[slot], hThi[slot][:, 0:KP].bitcast(F32), ALU.subtract).then_inc(lo_ready, 1)

                    def compare(g, par, r):
                        dve.wait_ge(held, g + 1)
                        for a in range(QUAD):
                            dve.wait_ge(got[par][a], 16 * r + 16)
                        nc.vector.tensor_copy(wedge[:, ds(QUAD * H * g, QUAD * H)], gst[par].rearrange("p a h -> p (a h)"))
                        nc.vector.tensor_copy(isg[par], src_e[:, ds(QUAD * g + 2 * QUAD, QUAD)]).then_inc(idx_ready, 1)
                        dve.wait_ge(spread, g + 1)

                        def pair(t, b):
                            nc.vector.tensor_scalar(onehotT[b][:, :], ps[4 + par][:, :], node_mid[:, ds(t, 1)], None, ALU.is_equal).then_inc(ohT_ready, 1)

                        def second(t, c):
                            dve.wait_ge(picked, c)
                            pair(t, 2)

                        def later(t, c):
                            dve.wait_ge(picked, c + 1)
                            pair(t, 2)
                        tiles_of(dve, g, lambda t, c: pair(t, par), second, later)
                        dve.drain().then_inc(spread_free, 1)

                    def collect(g, par):
                        dve.wait_ge(pick_done, g + 1)
                        nc.vector.tensor_reduce(picked_e[:, ds(g * QUAD * 2 * H, QUAD * 2 * H)].rearrange("p (a j) -> p a j", a=QUAD),
                                                ps[6 + par][:, 0:QUAD * 6 * H].rearrange("p (a s j) -> p a j s", a=QUAD, s=3),
                                                AX.X, ALU.add).then_inc(pick_free, 1)

                    def tq(g, par, i, s, slot, r):
                        if s == 3 and not (isinstance(i, int) and i == NT - 1):
                            split_lo(i + 1, 1 - slot)
                        compare(g, par, 4 * r + 2 * slot + s // 2)
                        collect(g, 1 - par)

                    for par in range(2):
                        nc.vector.tensor_copy(isg[par], src_e[:, par * QUAD:(par + 1) * QUAD]).then_inc(idx_ready, 1)
                    dve.drain().then_inc(spread_free, 2)
                    dve.drain().then_inc(pick_free, 1)
                    dve.drain().then_inc(lo_ready, 1)
                    split_lo(0, 0)
                    schedule(dve, tq, lambda g, par: (compare(g, par, g // 2), collect(g, 1 - par)))
                    collect(G, 1)

                @block.tensor
                def _(pe):
                    pe.drain().then_inc(picked, 1)
                    pe.drain().then_inc(sliced, QUAD)

                    def spread_targets(g, par):
                        pe.wait_ge(spread_free, g + 1)
                        nc.tensor.matmul(ps[4 + par][:, :], ident_h[0:G, ds(g, 1)].to_broadcast([G, P]),
                                         q_dst[0:G, :], start=True, stop=True).then_inc(spread, 1)

                    def pick(g, par):
                        pe.wait_ge(pick_free, g + 1)
                        bank = ps[6 + par]
                        nc.tensor.matmul(bank[:, 0:QUAD * 6 * H], zeros[:, 0:P], zeros[:, 0:QUAD * 6 * H], start=True, stop=False, skip_group_check=True)

                        def pair(t, c, b):
                            pe.wait_ge(ohT_ready, c + 1)
                            for a in range(QUAD):
                                last = nc.tensor.matmul(bank[:, a * 6 * H:(a + 1) * 6 * H], onehotT[b][:, a * P:(a + 1) * P],
                                                        own_b[:, ds(t * 6 * H, 6 * H)], start=False, stop=False, skip_group_check=True)
                            last.then_inc(picked, 1)
                        tiles_of(pe, g, lambda t, c: pair(t, c, par), lambda t, c: pair(t, c, 2))
                        nc.tensor.matmul(bank[:, 0:QUAD * 6 * H], zeros[:, 0:P], zeros[:, 0:QUAD * 6 * H], start=False, stop=True,
                                         skip_group_check=True).then_inc(pick_done, 1)

                    def tq(g, par, i, s, slot, r):
                        spread_targets(g + 1, 1 - par)
                        if s == 0:
                            pe.wait_ge(lo_ready, i + 2)
                        pe.wait_ge(evac, g + 1)
                        m = 0
                        for a, w in ((hThi, whi), (hThi, wlo), (hTlo, whi)):
                            for k in range(K):
                                last = nc.tensor.matmul(ps[s][:, 0:SW], a[slot][:, k * P:(k + 1) * P],
                                                        w[:, k * 2 * W + s * SW:k * 2 * W + (s + 1) * SW],
                                                        start=(m == 0), stop=(m == 3 * K - 1))
                                m += 1
                        last.then_inc(sliced, 1)
                        pick(g, par)

                    def plain(g, par):
                        if g + 1 < G:
                            spread_targets(g + 1, 1 - par)
                        pick(g, par)
                    nc.tensor.matmul(ps[7][:, 0:QUAD * 6 * H], zeros[:, 0:P], zeros[:, 0:QUAD * 6 * H], start=True, stop=True).then_inc(pick_done, 1)
                    spread_targets(0, 0)
                    schedule(pe, tq, plain)

        def softmax_weights(layer, n, aux):
            H = layer.H
            NA = 6 * H + 1
            picked_e = arena[:, 4096 + QUAD * 2 * H:4096 + (TE + QUAD) * 2 * H].rearrange("p (k j) -> p k j", j=2 * H)
            source = wedge[:, 0:TE * H].rearrange("p (k h) -> p k h", h=H)
            eb = arena[:, 7456:7456 + H * 512].rearrange("p (h k) -> p h k", h=H)[:, :, 0:TE]
            logit = eb.rearrange("p h k -> p k h")
            up = arena[0:G, 2048:2048 + H * QE].rearrange("p (h e) -> p h e", h=H)
            top = arena[0:G, 0:H * QE].rearrange("p (h e) -> p h e", h=H)
            row = arena[0:H, 2048:2048 + 4 * P]
            edge_max = arena[:, 9504:9504 + TE * H].rearrange("p (k h) -> p k h", h=H)
            carry = arena[0:G, 11168:11168 + 8]
            pen = lambda b: pens[0:G, b * QE:(b + 1) * QE]
            dve_steps, pe_steps = sem(f"sm{n}_dve"), sem(f"sm{n}_pe")
            with nc.Block() as block:
                @block.vector
                def _(dve):
                    nc.vector.tensor_tensor(logit, source, picked_e[:, :, 0:H], ALU.add)
                    dve.drain()
                    nc.vector.scalar_tensor_tensor(eb, eb, 0.2, eb, ALU.mult, ALU.max).then_inc(dve_steps, 1)
                    for h in range(H):
                        dve.wait_ge(pe_steps, h + 1)
                        nc.vector.tensor_tensor_scan(up[:, h, :], pen(0), ps[h][0:G, :], -BIG, ALU.add, ALU.max)
                        dve.drain()
                        nc.vector.tensor_tensor_scan(top[:, h, ::-1], pen(1)[:, ::-1], up[:, h, ::-1], -BIG, ALU.add, ALU.max).then_inc(dve_steps, 1)
                    dve.wait_ge(pe_steps, H + 1)
                    S, R, CF, CB = [row[:, b * P:b * P + G] for b in range(4)]
                    rp = lambda b: rpens[0:H, b * P:b * P + G]
                    nc.vector.tensor_tensor_scan(S, rp(0), ps[4][0:H, 0:G], -BIG, ALU.add, ALU.max)
                    nc.vector.tensor_tensor_scan(R[:, ::-1], rp(1)[:, ::-1], ps[4][0:H, P:P + G][:, ::-1], -BIG, ALU.add, ALU.max)
                    nc.vector.memset(CF[:, 0:1], -BIG)
                    nc.vector.memset(CB[:, G - 1:G], -BIG)
                    dve.drain()
                    nc.vector.tensor_tensor(CF[:, 1:G], S[:, 0:G - 1], rp(2)[:, 1:G], ALU.add)
                    nc.vector.tensor_tensor(CB[:, 0:G - 1], R[:, 1:G], rp(3)[:, 0:G - 1], ALU.add).then_inc(dve_steps, 1)
                    dve.wait_ge(pe_steps, H + 2)
                    nc.vector.tensor_copy(carry, ps[5][0:G, 0:8])
                    dve.drain()
                    for d in range(2):
                        for h in range(H):
                            last = nc.vector.scalar_tensor_tensor(top[:, h, :], pen(2 + d), carry[:, 4 * d + h:4 * d + h + 1],
                                                                  top[:, h, :], ALU.add, ALU.max)
                        dve.drain().then_inc(dve_steps, 1)
                    for h in range(H):
                        dve.wait_ge(pe_steps, H + 3 + h)
                        nc.vector.tensor_tensor(edge_max[:, :, h].rearrange("p (g a) -> p g a", a=QUAD),
                                                ps[h][:, :].rearrange("p (a g) -> p g a", a=QUAD)[:, 0:G, :],
                                                picked_e[:, :, H + h].rearrange("p (g a) -> p g a", a=QUAD), ALU.max)

                @block.tensor
                def _(pe):
                    pe.wait_ge(dve_steps, 1)
                    for h in range(H):
                        for a in range(QUAD):
                            last = nc.tensor.transpose(ps[h][0:G, a * P:(a + 1) * P],
                                                       eb[:, h, :].rearrange("p (g a) -> p g a", a=QUAD)[:, :, a], ident[:, :])
                        last.then_inc(pe_steps, 1)
                    pe.wait_ge(dve_steps, 1 + H)
                    nc.tensor.transpose(ps[4][0:H, 0:G], top[:, :, QE - 1], ident[0:G, 0:G])
                    nc.tensor.transpose(ps[4][0:H, P:P + G], top[:, :, 0], ident[0:G, 0:G]).then_inc(pe_steps, 1)
                    pe.wait_ge(dve_steps, H + 2)
                    nc.tensor.matmul(ps[5][:, 0:8], zeros[:, 0:P], zeros[:, 0:8], start=True, stop=True)
                    for d in range(2):
                        last = nc.tensor.transpose(ps[5][0:G, 4 * d:4 * d + H], row[:, (2 + d) * P:(2 + d) * P + G], ident[0:H, 0:H])
                    last.then_inc(pe_steps, 1)
                    pe.wait_ge(dve_steps, H + 4)
                    for h in range(H):
                        for a in range(QUAD):
                            last = nc.tensor.transpose(ps[h][:, a * P:a * P + G], top[:, h, a * P:(a + 1) * P], ident[0:G, 0:G])
                        last.then_inc(pe_steps, 1)

            search_maxima(layer, n, eb, edge_max)

            both = arena[:, 0:TE * 2 * H].rearrange("p (k j) -> p k j", j=2 * H)
            rest = arena[:, 4096:4096 + TE * 2 * H].rearrange("p (k j) -> p k j", j=2 * H)
            parts = aux[:, 0:TE * NA].rearrange("p (k c) -> p k c", c=NA)
            part = lambda s: parts[:, :, s * 2 * H:(s + 1) * 2 * H]
            z_ready, w_ready, p0, r0, p1 = [sem(f"sm{n}_{m}") for m in "z w p0 r0 p1".split()]
            with nc.Block() as block:
                @block.vector
                def _(dve):
                    nc.vector.tensor_tensor(both[:, :, 0:H], logit, edge_max, ALU.subtract)
                    nc.vector.tensor_tensor(both[:, :, H:2 * H], picked_e[:, :, H:2 * H], edge_max, ALU.subtract).then_inc(z_ready, 1)
                    dve.wait_ge(p0, 1)
                    nc.vector.tensor_tensor(rest, both, part(0), ALU.subtract).then_inc(r0, 1)
                    dve.wait_ge(p1, 1)
                    nc.vector.tensor_tensor(part(2), rest, part(1), ALU.subtract)

                @block.scalar
                def _(act):
                    act.wait_ge(z_ready, 1)
                    nc.scalar.activation(both, both, ACT.Exp).then_inc(w_ready, 1)
                    act.wait_ge(w_ready, 1)
                    nc.scalar.activation(part(0), both, ACT.Copy).then_inc(p0, 1)
                    nc.scalar.activation(source, both[:, :, 0:H], ACT.Copy)
                    act.wait_ge(r0, 1)
                    nc.scalar.activation(part(1), rest, ACT.Copy).then_inc(p1, 1)

                @block.gpsimd
                def _(pool):
                    pool.memset(parts[:, :, 6 * H:NA], 1.0)
                    pool.memset(aux[:, TE * NA:TCOL * NA], 0.0)

        def search_maxima(layer, n, eb, edge_max):
            H = layer.H
            stage = arena[0:G, 0:H * QE]
            quad_log = arena[:, 0:H * QE].rearrange("p (h e) -> p h e", h=H)
            quad_dst = arena[:, 2048:2048 + QE]
            other = arena[:, 2560:2560 + QE]
            masked = arena[:, 3072:3072 + QE]
            node_max = arena[:, 3584:3584 + NT * H]
            best = arena[:, 3700:3701]
            idx = arena[:, 3704:3705].bitcast(I32)
            found = arena[:, 3712:3712 + H]
            (eT, staged, e_out, quad_in, compared, nm_ready, nm_out, idx_ready, found_in) = fb_sems
            e_out0, quad0, compared0, edge0 = n * 16 * (L1.H + 1), n * G, n * (G + 1), n * TE

            def when_unsorted(eng, body):
                unsorted = eng.value_load(uns_i[0:1, 0:1], min_val=0, max_val=1)
                with eng.If(unsorted > 0):
                    body()

            with nc.Block() as block:
                @block.tensor
                def _(pe):
                    def body():
                        for h in range(H):
                            for a in range(QUAD):
                                last = nc.tensor.transpose(ps[h][0:G, a * P:(a + 1) * P],
                                                           eb[:, h, :].rearrange("p (g a) -> p g a", a=QUAD)[:, :, a], ident[:, :])
                        last.then_inc(eT, 1)
                    when_unsorted(pe, body)

                @block.vector
                def _(dve):
                    def body():
                        dve.wait_ge(eT, n + 1)
                        for h in range(H):
                            nc.vector.tensor_copy(stage[:, h * QE:(h + 1) * QE], ps[h][0:G, :])
                        nc.vector.tensor_copy(quad_dst[0:G, :], q_dst[0:G, :])
                        nc.vector.tensor_copy(node_max.rearrange("p (t h) -> p t h", h=H),
                                              own_log[:, 0:NT * 2 * H].rearrange("p (t j) -> p t j", j=2 * H)[:, :, H:2 * H])
                        dve.drain().then_inc(staged, 1)
                        with dve.Fori(0, G) as g:
                            dve.wait_ge(quad_in, 32 * (g + quad0) + 32)
                            nc.vector.tensor_copy(best, quad_dst[:, 0:1])
                            dve.drain()
                            with dve.Fori(0, NT) as t:
                                nc.vector.tensor_scalar(other, quad_dst, node_mid[:, ds(t, 1)], None, ALU.is_equal)
                                dve.drain()
                                nc.vector.tensor_scalar(other, other, -1.0, BIG, ALU.add, ALU.mult)
                                dve.drain()
                                for h in range(H):
                                    nc.vector.tensor_tensor(masked, quad_log[:, h, :], other, ALU.add)
                                    dve.drain()
                                    nc.vector.tensor_reduce(best, masked, AX.X, ALU.max)
                                    dve.drain()
                                    nm = node_max[:, ds(t * H + h, 1)]
                                    nc.vector.tensor_tensor(nm, nm, best, ALU.max)
                                    dve.drain()
                            dve.drain().then_inc(compared, 1)
                        dve.drain().then_inc(nm_ready, 1)
                        with dve.Fori(0, TE) as k:
                            nc.vector.tensor_scalar(idx, dst_e[:, ds(k, 1)], 0.0, None, ALU.max).then_inc(idx_ready, 1)
                            dve.wait_ge(found_in, 16 * (k + edge0) + 16)
                            nc.vector.tensor_tensor(edge_max[:, ds(k, 1), :].rearrange("p k h -> p (k h)"), found,
                                                    eb[:, :, ds(k, 1)].rearrange("p h k -> p (h k)"), ALU.max)
                            dve.drain()
                    when_unsorted(dve, body)

                @block.sync
                def _(sp):
                    def body():
                        sp.wait_ge(staged, n + 1)
                        for h in range(H):
                            sp.dma_start(quad_d[:, h, :], stage[:, h * QE:(h + 1) * QE]).then_inc(e_out, 16)
                        sp.dma_start(quad_d[:, 4, :], quad_dst[0:G, :]).then_inc(e_out, 16)
                        sp.wait_ge(e_out, e_out0 + 16 * (H + 1))
                        sp.drain().then_inc(compared, 1)
                        with sp.Fori(0, G) as g:
                            sp.wait_ge(compared, g + compared0 + 1)
                            sp.dma_start(quad_log, quad_d[ds(g, 1), 0:H, :].rearrange("g h e -> (g h) e").partition_broadcast(P)).then_inc(quad_in, 16)
                            sp.dma_start(quad_dst, quad_d[ds(g, 1), 4, :].rearrange("g e -> (g e)").partition_broadcast(P)).then_inc(quad_in, 16)
                        sp.wait_ge(nm_ready, n + 1)
                        sp.dma_start(max_d[n].rearrange("(t p) h -> p t h", p=P), node_max.rearrange("p (t h) -> p t h", h=H),
                                     allow_slow_non_contiguous=True).then_inc(nm_out, 16)
                        sp.wait_ge(nm_out, 16 * n + 16)
                    when_unsorted(sp, body)

                @block.gpsimd
                def _(pool):
                    def body():
                        pool.wait_ge(nm_out, 16 * n + 16)
                        with pool.Fori(0, TE) as k:
                            pool.wait_ge(idx_ready, k + edge0 + 1)
                            hold(pool)
                            pool.drain()
                            pool.indirect_dma_start(out=found, out_offset=None, in_=max_d[n][:, :],
                                                    in_offset=bass.IndirectOffsetOnAxis(ap=idx, axis=0)).then_inc(found_in, 16)
                    when_unsorted(pool, body)

        def aggregate(layer, n, aux):
            H, W, C = layer.H, layer.W, layer.C
            NA = 6 * H + 1
            first = n == 0
            gbuf = [arena[:, a * 1024:a * 1024 + W] for a in range(QUAD)]
            wone = arena[:, 4096:4096 + QUAD * H * P].rearrange("p (a h d) -> p a h d", a=QUAD, h=H)
            onehot = arena[:, 6144:6400].bitcast(BF16).rearrange("p (a d) -> p a d", a=QUAD)
            iota_t = arena[:, 6400:6528]
            own, rr, o = [arena[:, c:c + W] for c in (6528, 7552, 8576)]
            xr = arena[:, 9600:9600 + W]
            hTs = arena[:, 9600:10624]
            small = arena[:, 10624:11264]
            isg = small[:, 64:64 + QUAD].bitcast(I32)
            stat = small[:, 80:112]
            sums = small[:, 112:112 + 2 * H]
            cnt = small[:, 128:130]
            den_s = small[:, 132:132 + H]
            logits2 = small[0:2, 160:160 + P]
            unused = small[:, 300:300 + QUAD]
            wself = small[:, 136:136 + H]
            agg = [[ps[0], ps[1]], [ps[2], ps[3]]]
            den = [ps[4][:, 0:NA], ps[5][:, 0:NA]]
            pH = (ps[6], ps[7])
            pL = ps[6][0:2, 0:P]
            got = [sem(f"ag{n}_got{a}") for a in range(QUAD)]
            (onehot_ready, wone_ready, used, idx_ready, agg_done, agg_free, epi_done, rows_in, vec_in, scaled,
             var_ready, inv_ready, nb_ready) = [
                sem(f"ag{n}_{m}") for m in "oh wone used idx agg_done agg_free epi rows vec scaled var inv nb".split()]
            if first:
                scaled_ready, rr_ready, h1T, hTs_ready, hT_out, logit, logits_ready = [
                    sem(f"ag{n}_{m}") for m in "scaled_oh rr h1T hTs hT_out logit logits".split()]
            else:
                out_done = sem(f"ag{n}_out_done")
            ROWS = 2 if first else 3
            DVE_HEADS = H - 1 if first else H

            def start(k):
                return nc.s_assert_within(k, 0, TE, skip_runtime_bounds_check_because=
                                          "every group of a node tile starts in front of its last edge tile")

            def groups(eng, t, tile, between=None, steps=None):
                lo = eng.value_load(lo_i[0:1, ds(t, 1)], min_val=0, max_val=TE)
                count = eng.value_load(groups_i[0:1, ds(t, 1)], min_val=1, max_val=G)
                off = eng.value_load(off_i[0:1, ds(t, 1)], min_val=0, max_val=G * NT)

                def group(k, q, pause=None):
                    for a in range(QUAD):
                        tile(k + a, q, a)
                        if pause:
                            pause(a)

                def others(begin):
                    with eng.Fori(begin, count) as j:
                        group(start(lo + QUAD * j), off + j)
                if not between and not steps:
                    others(0)
                    return
                group(lo, off)
                if between:
                    between()
                    with eng.If(count > 1):
                        others(1)
                    return
                with eng.If(count < 2):
                    for step in steps:
                        step()
                with eng.If(count > 1):
                    with eng.If(count < 3):
                        group(start(lo + QUAD), off + 1, lambda a: steps[a]())
                    with eng.If(count > 2):
                        group(start(lo + QUAD), off + 1, lambda a: a % 2 == 0 and steps[a // 2]())
                        group(start(lo + 2 * QUAD), off + 2, lambda a: a % 2 == 0 and steps[2 + a // 2]())
                        with eng.If(count > 3):
                            others(3)

            with nc.Block() as block:
                @block.gpsimd
                def _(pool):
                    def tile(k, q, a):
                        pool.wait_ge(used, QUAD * q + a + 1)
                        pool.tensor_copy(isg[:, a:a + 1], src_e[:, ds(k, 1)]).then_inc(idx_ready, 1)
                        pool.wait_ge(idx_ready, QUAD * q + a + 1)
                        hold(pool, a)
                        pool.indirect_dma_start(out=gbuf[a], out_offset=None, in_=xl_d[n][:, :],
                                                in_offset=bass.IndirectOffsetOnAxis(ap=isg[:, a:a + 1], axis=0)).then_inc(got[a], 16)

                    def residual(t):
                        pool.wait_ge(rows_in, 16 * ROWS * (t + 1))
                        pool.tensor_tensor(rr, rr, vec[:, 3072:3072 + W], ALU.add).then_inc(rr_ready, 1)
                    if first:
                        pool.wait_ge(vec_in, 64)
                        groups(pool, 0, tile)
                        with pool.Fori(1, NT) as t:
                            groups(pool, t, tile, between=lambda: residual(t - 1))
                        residual(NT - 1)
                    else:
                        with pool.Fori(0, NT) as t:
                            groups(pool, t, tile)

                @block.scalar
                def _(act):
                    nc.scalar.preload_act_table_set("natural_log_exp_and_others")
                    if first:
                        act.drain().then_inc(hT_out, 32)

                    def tile(k, q, a):
                        if DVE_HEADS < H:
                            act.wait_ge(onehot_ready, QUAD * q + a + 1)
                            nc.scalar.activation(unused[:, a:a + 1], ident[:, 0:1], ACT.Copy)
                            for h in range(DVE_HEADS, H):
                                last = nc.scalar.activation(wone[:, a, h, :], onehot[:, a, :], ACT.Copy, scale=wedge[:, ds(k * H + h, 1)])
                            last.then_inc(scaled_ready, 1)

                    def post(t):
                        act.wait_ge(hT_out, 32 * t + 32)
                        for b in range(2):
                            act.wait_ge(h1T, 2 * t + 3 + b)
                            nc.scalar.activation(hTs[:, b * 512:(b + 1) * 512], pH[b][:, :], ACT.Copy).then_inc(hTs_ready, 1)
                        act.wait_ge(logit, t + 1)
                        nc.scalar.activation(logits2, pL, ACT.Copy).then_inc(logits_ready, 1)

                    def invert(t):
                        act.wait_ge(var_ready, t + 1)
                        inverse_root(act, stat).then_inc(inv_ready, 1)

                    def normalise(t):
                        act.wait_ge(nb_ready, t + 1)
                        nc.scalar.activation(o, o, ACT.Identity, scale=stat[:, 14:15], bias=stat[:, 15:16]).then_inc(scaled, 1)

                    def steps(t):
                        return [lambda: None, lambda: invert(t), lambda: normalise(t), lambda: None]

                    if first:
                        groups(act, 0, tile)
                        with act.Fori(1, NT) as t:
                            groups(act, t, tile, steps=steps(t - 1))
                            post(t - 1)
                        for step in steps(NT - 1):
                            step()
                        post(NT - 1)
                    else:
                        with act.Fori(0, NT) as t:
                            invert(t)
                            normalise(t)

                @block.vector
                def _(dve):
                    def tile(k, q, a):
                        dve.wait_ge(used, QUAD * q + a + 1)
                        nc.vector.tensor_scalar(onehot[:, a, :], iota_t, dst_e[:, ds(k, 1)], None, ALU.is_equal).then_inc(onehot_ready, 1)
                        for h in range(DVE_HEADS):
                            last = nc.vector.tensor_scalar(wone[:, a, h, :], iota_t, dst_e[:, ds(k, 1)],
                                                           wedge[:, ds(k * H + h, 1)], ALU.is_equal, ALU.mult)
                        last.then_inc(wone_ready, 1)

                    def nodes(t):
                        dve.drain()
                        nc.vector.tensor_scalar(iota_t, iota[:, :], tbase[:, ds(t, 1)], None, ALU.add)
                        dve.drain()

                    ws = lambda h: wself[:, h:h + 1]
                    rs = lambda h: den_s[:, h:h + 1]
                    part = lambda ap, h: ap[:, h * C:(h + 1) * C]

                    def sum_up(t, par):
                        dve.wait_ge(agg_done, t + 1)
                        nc.vector.tensor_reduce(sums, den[par][:, 0:6 * H].rearrange("p (s j) -> p j s", s=3), AX.X, ALU.add)
                        nc.vector.tensor_scalar(cnt[:, 0:1], den[par][:, 6 * H:NA], 1.0, None, ALU.max)
                        nc.vector.tensor_scalar(cnt[:, 1:2], den[par][:, 6 * H:NA], 0.0, None, ALU.is_equal)
                        dve.drain()
                        nc.vector.reciprocal(cnt[:, 0:1], cnt[:, 0:1])
                        dve.drain()
                        nc.vector.tensor_scalar(wself, sums[:, H:2 * H], cnt[:, 1:2], cnt[:, 0:1], ALU.add, ALU.mult)
                        dve.drain()
                        nc.vector.tensor_tensor(den_s, wself, sums[:, 0:H], ALU.add)
                        dve.wait_ge(rows_in, 16 * ROWS * (t + 1))
                        if first:
                            dve.wait_ge(h1T, 2 * t + 2)
                        else:
                            dve.wait_ge(out_done, 16 * t + 16)
                        if first:
                            for h in range(H):
                                last = nc.vector.scalar_tensor_tensor(part(o, h), part(own, h), ws(h),
                                                                      agg[par][h // 2][:, (h % 2) * C:(h % 2 + 1) * C], ALU.mult, ALU.add)
                        else:
                            nc.vector.scalar_tensor_tensor(o[:, 0:512], own[:, 0:512], ws(0), agg[par][0][:, 0:512], ALU.mult, ALU.add)
                            last = nc.vector.scalar_tensor_tensor(o[:, 512:W], own[:, 512:W], ws(0), agg[par][1][:, 0:W - 512], ALU.mult, ALU.add)
                        last.then_inc(agg_free, 1)

                    def divide(t):
                        dve.drain()
                        nc.vector.tensor_scalar(den_s, den_s, 1e-16, None, ALU.add)
                        dve.drain()
                        nc.vector.reciprocal(den_s, den_s)
                        dve.drain()
                        for h in range(H):
                            nc.vector.scalar_tensor_tensor(part(o, h), part(o, h), rs(h), part(vec[:, 0:W], h), ALU.mult, ALU.add)
                        dve.drain()
                        for b in range(2):
                            nc.vector.bn_stats(stat[:, 6 * b:6 * b + 6], o[:, b * W // 2:(b + 1) * W // 2])
                        dve.drain()
                        nc.vector.bn_aggr(stat[:, 12:14], stat[:, 0:12])
                        dve.drain()
                        nc.vector.tensor_scalar(stat[:, 13:14], stat[:, 13:14], EPS, None, ALU.add).then_inc(var_ready, 1)

                    def refine(t):
                        dve.wait_ge(inv_ready, t + 1)
                        newton(dve, stat)
                        nc.vector.scalar_tensor_tensor(stat[:, 15:16], stat[:, 12:13], -1.0, stat[:, 14:15], ALU.mult, ALU.mult).then_inc(nb_ready, 1)

                    def finish(t):
                        dve.wait_ge(scaled, t + 1)
                        nc.vector.tensor_tensor(o, o, vec[:, 1024:1024 + W], ALU.mult)
                        dve.drain()
                        nc.vector.tensor_tensor(o, o, vec[:, 2048:2048 + W], ALU.add)
                        if first:
                            dve.drain()
                            dve.wait_ge(rr_ready, t + 1)
                            nc.vector.scalar_tensor_tensor(o, o, 0.0, rr, ALU.max, ALU.add).then_inc(epi_done, 1)
                        else:
                            nc.vector.tensor_tensor(rr, rr, xr, ALU.add)
                            dve.drain()
                            nc.vector.tensor_tensor(o, o, rr, ALU.add).then_inc(epi_done, 1)

                    def epilogue(t, par):
                        return [lambda: sum_up(t, par), lambda: divide(t), lambda: refine(t), lambda: finish(t)]

                    dve.drain().then_inc(agg_free, 2)
                    dve.wait_ge(vec_in, 64)
                    if not first:
                        nc.vector.tensor_tensor(vec[:, 2048:2048 + W], vec[:, 2048:2048 + W], vec[:, 3072:3072 + W], ALU.add)
                    nodes(0)
                    groups(dve, 0, tile)
                    with dve.Fori(0, NT // 2) as r:
                        for par in range(2):
                            t = 2 * r + 1 + par
                            nodes(t)
                            groups(dve, t, tile, steps=epilogue(t - 1, par))
                    for step in epilogue(NT - 1, 0):
                        step()

                @block.tensor
                def _(pe):
                    pe.drain().then_inc(used, QUAD)
                    if first:
                        pe.drain().then_inc(h1T, 2)

                    def zero(par, start):
                        for b, w in ((agg[par][0], 512), (agg[par][1], W - 512), (den[par], NA)):
                            w = w if start else 1
                            last = nc.tensor.matmul(b[:, 0:w], zeros[:, 0:P], zeros[:, 0:w], start=start, stop=not start, skip_group_check=True)
                        return last

                    def node_tile(t, par):
                        def tile(k, q, a):
                            pe.wait_ge(wone_ready, QUAD * q + a + 1)
                            pe.wait_ge(got[a], 16 * q + 16)
                            if first:
                                for h in range(H):
                                    if h == DVE_HEADS:
                                        pe.wait_ge(scaled_ready, QUAD * q + a + 1)
                                    nc.tensor.matmul(agg[par][h // 2][:, (h % 2) * C:(h % 2 + 1) * C], wone[:, a, h, :],
                                                            gbuf[a][:, h * C:(h + 1) * C], start=False, stop=False, skip_group_check=True)
                            else:
                                nc.tensor.matmul(agg[par][0][:, 0:512], wone[:, a, 0, :], gbuf[a][:, 0:512], start=False, stop=False, skip_group_check=True)
                                nc.tensor.matmul(agg[par][1][:, 0:W - 512], wone[:, a, 0, :], gbuf[a][:, 512:W], start=False, stop=False, skip_group_check=True)
                            nc.tensor.matmul(den[par], onehot[:, a, :], aux[:, ds(k * NA, NA)],
                                             start=False, stop=False, skip_group_check=True).then_inc(used, 1)
                        pe.wait_ge(agg_free, t + 1)
                        zero(par, True)
                        groups(pe, t, tile)
                        zero(par, False).then_inc(agg_done, 1)

                    def post(t):
                        pe.wait_ge(epi_done, t + 2)
                        for b in range(2):
                            for m in range(4):
                                k = 4 * b + m
                                last = nc.tensor.transpose(pH[b][:, m * P:(m + 1) * P], o[:, k * P:(k + 1) * P], ident[:, :])
                            last.then_inc(h1T, 1)
                        pe.wait_ge(hTs_ready, 2 * t + 2)
                        for k in range(L2.K):
                            last = nc.tensor.matmul(pL, wa[:, k * 8:k * 8 + 2], hTs[:, k * P:(k + 1) * P],
                                                    start=(k == 0), stop=(k == L2.K - 1))
                        last.then_inc(logit, 1)

                    node_tile(0, 0)
                    with pe.Fori(0, NT // 2) as r:
                        for par in range(2):
                            t = 2 * r + 1 + par
                            node_tile(t, 1 - par)
                            if first:
                                post(t - 1)
                    if first:
                        post(NT - 1)

                @block.sync
                def _(sp):
                    for i, v in enumerate(((b1, g1, be1, br1), (b2, g2, be2, br2))[n]):
                        sp.dma_start(vec[:, i * 1024:i * 1024 + layer.W], v.partition_broadcast(P)).then_inc(vec_in, 16)
                    sp.drain().then_inc(epi_done, 1)
                    if not first:
                        sp.drain().then_inc(out_done, 16)

                    def rows(t, count=P):
                        sp.wait_ge(epi_done, t + 1)
                        if not first:
                            sp.wait_ge(out_done, 16 * t + 16)
                        sp.dma_start(own, xl_d[n][ds(t * P, P), :]).then_inc(rows_in, 16)
                        sp.wait_ge(rows_in, 16 * (ROWS * t + 1))
                        sp.dma_start(rr, res_d[n][ds(t * P, P), :]).then_inc(rows_in, 16)
                        if not first:
                            sp.wait_ge(rows_in, 16 * (ROWS * t + 2))
                            sp.dma_start(xr[0:count, :], x[ds(t * P, count), :]).then_inc(rows_in, 16)

                    def store_hT(t):
                        sp.wait_ge(hTs_ready, 2 * t + 2)
                        sp.dma_start(hT_d[1][ds(t, 1), :, :].rearrange("a p n -> (a p) n"), hTs).then_inc(hT_out, 16)
                        sp.wait_ge(logits_ready, t + 1)
                        sp.dma_start(logit_d[ds(t, 1), :, :].rearrange("a j n -> (a j) n"), logits2).then_inc(hT_out, 16)

                    def store_out(t, count=P):
                        sp.wait_ge(epi_done, t + 2)
                        sp.dma_start(out[ds(t * P, count), :], o[0:count, :]).then_inc(out_done, 16)

                    if first:
                        rows(0)
                        with sp.Fori(1, NT) as t:
                            rows(t)
                            store_hT(t - 1)
                        store_hT(NT - 1)
                        sp.wait_ge(hT_out, 32 * (NT + 1))
                    else:
                        with sp.Fori(0, NT - 1) as t:
                            rows(t)
                            store_out(t)
                        rows(NT - 1, LAST)
                        store_out(NT - 1, LAST)
                        sp.wait_ge(out_done, 16 * (NT + 1))

        def attention(layer, n, between=None):
            logit_tables(layer, n)
            project(layer, n)
            with nc.sbuf_tensor(f"aux{n}", [P, TCOL * (6 * layer.H + 1)], BF16) as aux:
                softmax_weights(layer, n, aux)
                if between:
                    between()
                aggregate(layer, n, aux)

        setup()
        load_weights(L1, W1, Wr1, a_src1, a_dst1)
        norm_input()
        attention(L1, 0, lambda: load_weights(L2, W2, Wr2, a_src2, a_dst2))
        attention(L2, 1)


_INS = ["x", "src", "dst"] + ["L0_gnn_" + n for n in (
    "W1", "a_src1", "a_dst1", "b1", "g1", "be1", "Wr1", "br1",
    "W2", "a_src2", "a_dst2", "b2", "g2", "be2", "Wr2", "br2")]


def kernel(**inputs):
    import numpy as np
    import concourse.bacc as bacc
    from concourse.bass_utils import run_bass_kernel_spmd

    nc = bacc.Bacc("TRN2", target_bir_lowering=False, num_devices=1)
    arrays, args = {}, []
    for name in _INS:
        a = np.ascontiguousarray(inputs[name])
        arrays[f"in_{name}"] = a
        args.append(nc.dram_tensor(f"in_{name}", a.shape, mybir.dt.from_np(a.dtype), kind="ExternalInput").ap())
    out = nc.dram_tensor("out_0", (N, IN), F32, kind="ExternalOutput").ap()
    gnn_kernel(nc, *args, out)
    r = run_bass_kernel_spmd(nc, [arrays], core_ids=[0])
    return r.results[0]["out_0"]
```
